# Optimizing a Trainium2 kernel written in Bass

```python
import numpy as np
import jax
import jax.numpy as jnp

def _softmax(x, axis=-1):
    return jax.nn.softmax(x, axis=axis)

def _gelu(x):
    return jax.nn.gelu(x, approximate=True)

def _silu(x):
    return jax.nn.silu(x)

def _sigmoid(x):
    return jax.nn.sigmoid(x)

def _layernorm(x, axis=-1, eps=1e-05):
    m = jnp.mean(x, axis=axis, keepdims=True)
    v = jnp.var(x, axis=axis, keepdims=True)
    return (x - m) / jnp.sqrt(v + eps)

def _scatter_add(tgt, idx, src, axis=0):
    return tgt.at[idx].add(src)

def _segment_sum(src, seg, n):
    return jax.ops.segment_sum(src, seg, n)
kernel_name = 'mk_dlrm_tower_d1_rec_r8_d9fd4c'

def setup_inputs(seed: int=0):
    np.random.seed(seed)
    _w = jnp.asarray

    def _rec_inputs():
        import jax
        import jax.numpy as jnp
        _tk = jax.random.key(seed)
        dense_ctx = jax.random.normal(jax.random.fold_in(_tk, 190), (2048, 16), jnp.float32)
        ids = jnp.stack([jax.random.randint(jax.random.fold_in(_tk, 200 + f), (2048,), 0, v, jnp.int32) for f, v in enumerate([1250, 1250, 125000, 1000, 1250, 12500, 12500, 1250, 12500, 1250, 12500, 12500, 1000, 1000, 1000, 12500, 1250, 1250, 1000, 1000, 1000, 1000, 12500, 12500, 1250, 1250, 1000])], axis=1)
        tbl_0 = 0.05 * jax.random.normal(jax.random.fold_in(_tk, 500 + 0), (1250, 128), jnp.float32)
        tbl_1 = 0.05 * jax.random.normal(jax.random.fold_in(_tk, 500 + 1), (1250, 128), jnp.float32)
        tbl_2 = 0.05 * jax.random.normal(jax.random.fold_in(_tk, 500 + 2), (125000, 128), jnp.float32)
        tbl_3 = 0.05 * jax.random.normal(jax.random.fold_in(_tk, 500 + 3), (1000, 128), jnp.float32)
        tbl_4 = 0.05 * jax.random.normal(jax.random.fold_in(_tk, 500 + 4), (1250, 128), jnp.float32)
        tbl_5 = 0.05 * jax.random.normal(jax.random.fold_in(_tk, 500 + 5), (12500, 128), jnp.float32)
        tbl_6 = 0.05 * jax.random.normal(jax.random.fold_in(_tk, 500 + 6), (12500, 128), jnp.float32)
        tbl_7 = 0.05 * jax.random.normal(jax.random.fold_in(_tk, 500 + 7), (1250, 128), jnp.float32)
        tbl_8 = 0.05 * jax.random.normal(jax.random.fold_in(_tk, 500 + 8), (12500, 128), jnp.float32)
        tbl_9 = 0.05 * jax.random.normal(jax.random.fold_in(_tk, 500 + 9), (1250, 128), jnp.float32)
        tbl_10 = 0.05 * jax.random.normal(jax.random.fold_in(_tk, 500 + 10), (12500, 128), jnp.float32)
        tbl_11 = 0.05 * jax.random.normal(jax.random.fold_in(_tk, 500 + 11), (12500, 128), jnp.float32)
        tbl_12 = 0.05 * jax.random.normal(jax.random.fold_in(_tk, 500 + 12), (1000, 128), jnp.float32)
        tbl_13 = 0.05 * jax.random.normal(jax.random.fold_in(_tk, 500 + 13), (1000, 128), jnp.float32)
        tbl_14 = 0.05 * jax.random.normal(jax.random.fold_in(_tk, 500 + 14), (1000, 128), jnp.float32)
        tbl_15 = 0.05 * jax.random.normal(jax.random.fold_in(_tk, 500 + 15), (12500, 128), jnp.float32)
        tbl_16 = 0.05 * jax.random.normal(jax.random.fold_in(_tk, 500 + 16), (1250, 128), jnp.float32)
        tbl_17 = 0.05 * jax.random.normal(jax.random.fold_in(_tk, 500 + 17), (1250, 128), jnp.float32)
        tbl_18 = 0.05 * jax.random.normal(jax.random.fold_in(_tk, 500 + 18), (1000, 128), jnp.float32)
        tbl_19 = 0.05 * jax.random.normal(jax.random.fold_in(_tk, 500 + 19), (1000, 128), jnp.float32)
        tbl_20 = 0.05 * jax.random.normal(jax.random.fold_in(_tk, 500 + 20), (1000, 128), jnp.float32)
        tbl_21 = 0.05 * jax.random.normal(jax.random.fold_in(_tk, 500 + 21), (1000, 128), jnp.float32)
        tbl_22 = 0.05 * jax.random.normal(jax.random.fold_in(_tk, 500 + 22), (12500, 128), jnp.float32)
        tbl_23 = 0.05 * jax.random.normal(jax.random.fold_in(_tk, 500 + 23), (12500, 128), jnp.float32)
        tbl_24 = 0.05 * jax.random.normal(jax.random.fold_in(_tk, 500 + 24), (1250, 128), jnp.float32)
        tbl_25 = 0.05 * jax.random.normal(jax.random.fold_in(_tk, 500 + 25), (1250, 128), jnp.float32)
        tbl_26 = 0.05 * jax.random.normal(jax.random.fold_in(_tk, 500 + 26), (1000, 128), jnp.float32)
        _rk = jax.random.fold_in(_tk, 7)
        W_top1 = 0.0521996 * jax.random.normal(jax.random.fold_in(_tk, 801), (367, 512), jnp.float32)
        W_top2 = 0.0441942 * jax.random.normal(jax.random.fold_in(_tk, 802), (512, 256), jnp.float32)
        W_top3 = 0.0625 * jax.random.normal(jax.random.fold_in(_tk, 803), (256, 1), jnp.float32)
        b_top1 = jnp.zeros((512,), jnp.float32)
        b_top2 = jnp.zeros((256,), jnp.float32)
        return (dense_ctx, ids, tbl_0, tbl_1, tbl_2, tbl_3, tbl_4, tbl_5, tbl_6, tbl_7, tbl_8, tbl_9, tbl_10, tbl_11, tbl_12, tbl_13, tbl_14, tbl_15, tbl_16, tbl_17, tbl_18, tbl_19, tbl_20, tbl_21, tbl_22, tbl_23, tbl_24, tbl_25, tbl_26, W_top1, b_top1, W_top2, b_top2, W_top3)
    dense_ctx, ids, tbl_0, tbl_1, tbl_2, tbl_3, tbl_4, tbl_5, tbl_6, tbl_7, tbl_8, tbl_9, tbl_10, tbl_11, tbl_12, tbl_13, tbl_14, tbl_15, tbl_16, tbl_17, tbl_18, tbl_19, tbl_20, tbl_21, tbl_22, tbl_23, tbl_24, tbl_25, tbl_26, W_top1, b_top1, W_top2, b_top2, W_top3 = _rec_inputs()

    def _L0_rec_setup():
        import jax, jax.numpy as jnp
        import numpy as np
        NUM_FEAS = 27
        key = jax.random.key(seed)
        inputs = jax.random.normal(key, (4096, NUM_FEAS, 128), dtype=jnp.float32)
        return {'inputs': inputs}
    _L0_rec_all = _L0_rec_setup()
    _L0_rec_in = {k: v for k, v in _L0_rec_all.items() if k in ()}
    del _L0_rec_all
    return {'dense_ctx': dense_ctx, 'ids': ids, 'tbl_0': tbl_0, 'tbl_1': tbl_1, 'tbl_2': tbl_2, 'tbl_3': tbl_3, 'tbl_4': tbl_4, 'tbl_5': tbl_5, 'tbl_6': tbl_6, 'tbl_7': tbl_7, 'tbl_8': tbl_8, 'tbl_9': tbl_9, 'tbl_10': tbl_10, 'tbl_11': tbl_11, 'tbl_12': tbl_12, 'tbl_13': tbl_13, 'tbl_14': tbl_14, 'tbl_15': tbl_15, 'tbl_16': tbl_16, 'tbl_17': tbl_17, 'tbl_18': tbl_18, 'tbl_19': tbl_19, 'tbl_20': tbl_20, 'tbl_21': tbl_21, 'tbl_22': tbl_22, 'tbl_23': tbl_23, 'tbl_24': tbl_24, 'tbl_25': tbl_25, 'tbl_26': tbl_26, 'W_top1': W_top1, 'b_top1': b_top1, 'W_top2': W_top2, 'b_top2': b_top2, 'W_top3': W_top3}

def reference(dense_ctx, ids, tbl_0, tbl_1, tbl_2, tbl_3, tbl_4, tbl_5, tbl_6, tbl_7, tbl_8, tbl_9, tbl_10, tbl_11, tbl_12, tbl_13, tbl_14, tbl_15, tbl_16, tbl_17, tbl_18, tbl_19, tbl_20, tbl_21, tbl_22, tbl_23, tbl_24, tbl_25, tbl_26, W_top1, b_top1, W_top2, b_top2, W_top3):
    import jax
    import jax.numpy as jnp

    def _L0_rec_ref(inputs):
        import jax, jax.numpy as jnp
        import numpy as np
        NUM_FEAS = 27
        n = inputs.shape[1]
        dot = jnp.einsum('bnd,bmd->bnm', inputs, inputs)
        iu, ju = jnp.triu_indices(n, k=1)
        return dot[:, iu, ju]
    e = jnp.stack([tbl_0[ids[:, 0]], tbl_1[ids[:, 1]], tbl_2[ids[:, 2]], tbl_3[ids[:, 3]], tbl_4[ids[:, 4]], tbl_5[ids[:, 5]], tbl_6[ids[:, 6]], tbl_7[ids[:, 7]], tbl_8[ids[:, 8]], tbl_9[ids[:, 9]], tbl_10[ids[:, 10]], tbl_11[ids[:, 11]], tbl_12[ids[:, 12]], tbl_13[ids[:, 13]], tbl_14[ids[:, 14]], tbl_15[ids[:, 15]], tbl_16[ids[:, 16]], tbl_17[ids[:, 17]], tbl_18[ids[:, 18]], tbl_19[ids[:, 19]], tbl_20[ids[:, 20]], tbl_21[ids[:, 21]], tbl_22[ids[:, 22]], tbl_23[ids[:, 23]], tbl_24[ids[:, 24]], tbl_25[ids[:, 25]], tbl_26[ids[:, 26]]], axis=1)
    z = _L0_rec_ref(e)
    z = z.reshape(z.shape[0], -1)
    h = jnp.concatenate([z, dense_ctx], axis=1)
    h = jnp.maximum(h @ W_top1 + b_top1, 0.0)
    h = jnp.maximum(h @ W_top2 + b_top2, 0.0)
    y = h @ W_top3
    return y

_drawn_inputs = setup_inputs


def setup_inputs(seed=0):
    import zlib

    import numpy as np

    out = dict(_drawn_inputs(seed))
    spreads = {'b_top1': (0.0, 0.1), 'b_top2': (0.0, 0.1)}
    factors = {}
    for name, (base, spread) in spreads.items():
        noise = np.random.default_rng([zlib.crc32(name.encode()), seed]).standard_normal(out[name].shape)
        drawn = base * np.exp(spread * noise) if base else spread * noise
        out[name] = jnp.asarray(drawn.astype(out[name].dtype))
    for name, factor in factors.items():
        out[name] = (out[name] * factor).astype(out[name].dtype)
    return out
```

```python
import numpy as np
import concourse.bass as bass
from concourse import mybir
from contextlib import ExitStack

BATCH = 2048
EMB = 128
CTX = 16
TABLE_ROWS = [1250, 1250, 125000, 1000, 1250, 12500, 12500, 1250, 12500, 1250, 12500, 12500, 1000, 1000,
              1000, 12500, 1250, 1250, 1000, 1000, 1000, 1000, 12500, 12500, 1250, 1250, 1000]
FEATS = len(TABLE_ROWS)
H1, H2 = 512, 256

SMALL = 1000
NO = 9
ONEHOT_TABLES = [f for f in range(FEATS) if TABLE_ROWS[f] == SMALL][:NO]
GATHER_TABLES = [f for f in range(FEATS) if f not in ONEHOT_TABLES]
NG = FEATS - NO
SLOTS = GATHER_TABLES + ONEHOT_TABLES
KROWS = 125
KCH = SMALL // KROWS

TILE = 128
CHUNK = 2 * TILE
BODY = 2 * CHUNK
TURNS = BATCH // BODY
TILES = BODY // TILE

RADIUS = (FEATS - 1) // 2
NB = 3
PAIRS = FEATS // NB * RADIUS
CTX_ROWS = 6
K1 = PAIRS + CTX_ROWS

def groups(total, count):
    sizes = [total // count + (g < total % count) for g in range(count)]
    return [(sum(sizes[:g]), sizes[g]) for g in range(count)]


GATHER_GROUPS = groups(NG, 5)
ONEHOT_GROUPS = groups(NO, 6 if NO > 8 else 4)


def pair_rows():
    iu = np.triu_indices(FEATS, k=1)
    row_of = {(a, b): k for k, (a, b) in enumerate(zip(*iu))}
    rows = np.full((NB, K1), -1)
    for b in range(NB):
        for q in range(PAIRS):
            n, r = b * (FEATS // NB) + q // RADIUS, 1 + q % RADIUS
            x, y = SLOTS[n], SLOTS[(n + r) % FEATS]
            rows[b, q] = row_of[(min(x, y), max(x, y))]
        for q in range(CTX_ROWS):
            if b * CTX_ROWS + q < CTX:
                rows[b, PAIRS + q] = len(iu[0]) + b * CTX_ROWS + q
    return rows


def build(nc, a):
    fp32, fp32r, i32 = mybir.dt.float32, mybir.dt.float32r, mybir.dt.int32
    ALU, ACT = mybir.AluOpType, mybir.ActivationFunctionType

    ctx = ExitStack()
    with ctx:
        def sb(name, shape, dt):
            return ctx.enter_context(nc.sbuf_tensor(name, shape, dt))

        def pb(name, shape, dt):
            return ctx.enter_context(nc.psum_tensor(name, shape, dt))

        def sem(name):
            return ctx.enter_context(nc.semaphore(name))

        def sems(name, n):
            return [sem(f"{name}{k}") for k in range(n)]

        SW = (FEATS + RADIUS) * 32
        OH_SLOTS, HALF = 3, KCH // 2
        table_hi = sb("table_hi", [KROWS, NO, KCH * EMB], fp32r)
        table_lo = sb("table_lo", [KROWS, NO, KCH * EMB], fp32r)
        gath = sb("gath", [TILE, TILES, NG, EMB], fp32)
        et = sb("et", [EMB, 2, TILE * 32], fp32)
        onehot = sb("onehot", [KROWS, OH_SLOTS, HALF, CHUNK], fp32r)
        idx = sb("idx", [TILE, TILES, NG], i32)
        ids_bc = sb("ids_bc", [KROWS, NO, CHUNK], i32)
        gram = sb("gram", [128, 2, FEATS * 32], fp32)
        samp = sb("samp", [TILE, 2, SW], fp32)
        prod = sb("prod", [TILE, 2, NB * PAIRS], fp32)
        zt = sb("zt", [K1, 2, NB, CHUNK], fp32)
        h1 = sb("h1", [128, H1 // 128, CHUNK], fp32)
        h2 = sb("h2", [128, H2 // 128, CHUNK], fp32)
        y_sb = sb("y_sb", [1, 2, CHUNK], fp32)
        w1 = sb("w1", [K1, NB, H1], fp32)
        w2 = sb("w2", [128, H1 // 128, H2], fp32)
        w3 = sb("w3", [128, H2 // 128], fp32)
        b1 = sb("b1", [128, H1 // 128], fp32)
        b2 = sb("b2", [128, H2 // 128], fp32)
        ident = sb("ident", [128, 128], fp32)
        rowno = sb("rowno", [KROWS, KCH], fp32)
        late = gath[0:KROWS, 2:TILES, :, :].rearrange("p k s d -> p (k s d)")
        raw = [samp[0:KROWS, 0, 0:KCH * EMB], samp[0:KROWS, 1, 0:KCH * EMB], h1[0:KROWS, :, :].rearrange("p m s -> p (m s)"),
               *(late[:, s * KCH * EMB:(s + 1) * KCH * EMB] for s in range(4))]
        RAWS = len(raw)

        EB = 4
        p_et = [pb(f"p_et{s}", [128, 512], fp32) for s in range(EB)]
        p_gram = [pb(f"p_gram{s}", [128, 512], fp32) for s in range(2)]
        p_mlp = [pb(f"p_mlp{s}", [128, 512], fp32) for s in range(2)]

        idx_loaded = sems("idx_loaded", TILES)
        bc_loaded = sem("bc_loaded")
        tiles_begun = sem("tiles_begun")
        gathered = [sems(f"gathered{k}_", len(GATHER_GROUPS)) for k in range(TILES)]
        raw_loaded = sems("raw_loaded", RAWS)
        const_loaded = sem("const_loaded")
        ident_loaded = sem("ident_loaded")
        weights_loaded = sem("weights_loaded")
        ctx_loaded = sems("ctx_loaded", 2)
        out_stored = sems("out_stored", 2)
        pad_zeroed = sem("pad_zeroed")
        hi_made = sem("hi_made")
        lo_made = sem("lo_made")
        oh_built = sems("oh_built", OH_SLOTS)
        oh_used = sems("oh_used", OH_SLOTS)
        chunk_built = sem("chunk_built")
        tile_transposed = sems("tile_transposed", TILES)
        et_filled = sem("et_filled")
        et_moved = sem("et_moved")
        gram_filled = sems("gram_filled", 2)
        gram_moved = sems("gram_moved", 2)
        gram_turned = sems("gram_turned", 2)
        samp_wrapped = sem("samp_wrapped")
        prod_ready = sems("prod_ready", 2)
        mlp_filled = sems("mlp_filled", 2)
        mlp_moved = sems("mlp_moved", 2)
        zt_ready = sem("zt_ready")
        h1_ready = sem("h1_ready")
        h2_ready = sem("h2_ready")
        y_ready = sems("y_ready", 2)

        NWEIGHTS = 5
        NOB, NTB = len(ONEHOT_GROUPS), len(GATHER_GROUPS)
        ET_TURN = 2 * (NOB + 2 * NTB)
        def et_tiles(i, half):
            return NOB + ET_TURN * i + half * (2 * NTB + NOB)

        def et_onehot(i, half):
            return ET_TURN * i + half * (2 * NTB + NOB)

        def bank_of_tile(half, k, g):
            return p_et[(et_tiles(0, half) + k * NTB + g) % EB]

        def bank_of_onehot(half, g):
            return p_et[(et_onehot(0, half) + g) % EB]

        UNITS = NO * 2 // OH_SLOTS
        assert ET_TURN % EB == 0
        GB = TILE // 16
        GRAMS = GB // 2

        block = ctx.enter_context(nc.Block())

        @block.sync
        def _(sp):
            def load_idx(i, k):
                sp.dma_start(idx[:, k, :], a["ids_gather"][bass.ds(i * TILES + k, 1), :, :].rearrange("o p f -> (o p) f")
                             ).then_inc(idx_loaded[k], 16)

            def load_bc(chunk):
                sp.dma_start(ids_bc[:, :, :], a["ids_onehot"][bass.ds(chunk, 1), :, :].to_broadcast([KROWS, NO, CHUNK])
                             ).then_inc(bc_loaded, 16)

            def load_raw(t):
                if t >= RAWS:
                    sp.wait_ge(lo_made, t - RAWS + 1)
                sp.dma_start(raw[t % RAWS], a["tables_onehot"][t]).then_inc(raw_loaded[t % RAWS], 16)

            for k in range(TILES):
                load_idx(0, k)
                if k == 0:
                    sp.dma_start(rowno[:, :], a["rowno"]).then_inc(const_loaded, 16)
                    load_bc(0)
                    load_raw(0)
                    load_raw(1)
            for t in range(2, NO):
                load_raw(t)

            def load_ctx(i, half):
                if not (isinstance(i, int) and i == 0):
                    sp.wait_ge(mlp_filled[1], 3 * (2 * i + half - 1) - 1)
                sp.dma_start(zt[PAIRS:K1, half, :, :], a["ctx"][bass.ds(2 * i + half, 1), :, :, :].rearrange("o q b s -> (o q) b s")
                             ).then_inc(ctx_loaded[half], 16)

            def store_y(i, half):
                sp.wait_ge(y_ready[half], i + 1)
                sp.dma_start(a["out"][bass.ds(2 * i + half, 1), :], y_sb[0:1, half, :]).then_inc(out_stored[half], 16)

            def turn(i, last):
                load_ctx(i, 0)
                sp.wait_ge(chunk_built, 2 * i + 1)
                load_bc(2 * i + 1)
                load_ctx(i, 1)
                if not last:
                    for k in (0, 1):
                        sp.wait_ge(tile_transposed[k], i + 1)
                        load_idx(i + 1, k)
                    sp.wait_ge(chunk_built, 2 * i + 2)
                    load_bc(2 * i + 2)
                store_y(i, 0)
                if not last:
                    for k in (2, 3):
                        sp.wait_ge(tile_transposed[k], i + 1)
                        load_idx(i + 1, k)
                store_y(i, 1)

            turn(0, False)
            with sp.Fori(1, TURNS - 1) as i:
                turn(i, False)
            turn(TURNS - 1, True)
            for half in (0, 1):
                sp.wait_ge(out_stored[half], 16 * TURNS)

        @block.gpsimd
        def _(pool):
            def turn(i):
                for k in range(TILES):
                    pool.wait_ge(idx_loaded[k], 16 * (i + 1))
                    if k == 2 and isinstance(i, int) and i == 0:
                        pool.wait_ge(lo_made, NO)
                    if not (isinstance(i, int) and i == 0):
                        pool.wait_ge(tile_transposed[k], i)
                    pool.sem_inc(tiles_begun, 1)
                    for g, (s0, n) in enumerate(GATHER_GROUPS):
                        for s in range(s0, s0 + n):
                            pool.indirect_dma_start(
                                gath[:, k, s, :], None, a[f"tbl_{GATHER_TABLES[s]}"],
                                bass.IndirectOffsetOnAxis(ap=idx[:, k, s:s + 1], axis=0),
                            ).then_inc(gathered[k][g], 16)

            turn(0)
            with pool.Fori(1, TURNS) as i:
                turn(i)

        @block.tensor
        def _(pe):
            def onehot_table(i, half, t):
                g = next(g for g, (t0, n) in enumerate(ONEHOT_GROUPS) if t0 <= t < t0 + n)
                t0, n = ONEHOT_GROUPS[g]
                u = et_onehot(i, half) + g
                bank = bank_of_onehot(half, g)
                if t == t0 and not (isinstance(u, int) and u < EB):
                    pe.wait_ge(et_moved, u - EB + 1)
                out = bank[:, (t - t0) * CHUNK:(t - t0 + 1) * CHUNK]
                for part in range(2):
                    v = 2 * t + part
                    pe.wait_ge(oh_built[v % OH_SLOTS], UNITS * (2 * i + half) + v // OH_SLOTS + 1)
                    for k in range(HALF):
                        kk = part * HALF + k
                        for tab in (table_hi, table_lo):
                            last = nc.tensor.matmul(out, tab[:, t, kk * EMB:(kk + 1) * EMB], onehot[:, v % OH_SLOTS, k, :],
                                                    start=(kk == 0 and tab is table_hi), stop=(kk == KCH - 1 and tab is table_lo))
                    last.then_inc(oh_used[v % OH_SLOTS], 1)

            def onehot_chunk(i, half, between):
                for t in range(NO):
                    if isinstance(i, int) and i == 0 and half == 0:
                        pe.wait_ge(lo_made, t + 1)
                    onehot_table(i, half, t)
                    if t in between:
                        between[t]()

            def transpose_tile(i, half, k):
                tile = 2 * half + k
                for g, (s0, n) in enumerate(GATHER_GROUPS):
                    u = et_tiles(i, half) + k * NTB + g
                    pe.wait_ge(gathered[tile][g], 16 * n * (i + 1))
                    pe.wait_ge(et_moved, u - EB + 1)
                    for s in range(s0, s0 + n):
                        last = nc.tensor.transpose(bank_of_tile(half, k, g)[:, (s - s0) * TILE:(s - s0 + 1) * TILE],
                                                   gath[:, tile, s, :], ident[:, :])
                    last.then_inc(tile_transposed[tile] if g == NTB - 1 else et_filled, 1)

            def gram_tile(i, half, k):
                pe.wait_ge(et_moved, et_tiles(i, half) + (k + 1) * NTB)
                for b in range(GB):
                    s = b % 2
                    n = GRAMS * (4 * i + 2 * half + k) + b // 2
                    if not (isinstance(n, int) and n == 0):
                        pe.wait_ge(gram_moved[s], n)
                    for q in range(4):
                        g = 4 * b + q
                        stat = et[:, k, 128 * g:128 * (g + 1)]
                        mov = stat.rearrange("p (j f) -> p j f", f=32)[:, :, 0:FEATS]
                        last = nc.tensor.matmul(p_gram[s][:, q * 4 * FEATS:(q + 1) * 4 * FEATS],
                                                stat, mov, start=True, stop=True)
                    last.then_inc(gram_filled[s], 1)

            def pairs(i, half):
                c = 2 * i + half
                for k in range(2):
                    pe.wait_ge(prod_ready[k], c + 1)
                    if not (isinstance(c, int) and c == 0):
                        pe.wait_ge(mlp_moved[k], 3 * c)
                    for b in range(NB):
                        last = nc.tensor.transpose(p_mlp[k][0:PAIRS, b * TILE:(b + 1) * TILE],
                                                   prod[:, k, b * PAIRS:(b + 1) * PAIRS], ident[:, :])
                    last.then_inc(mlp_filled[k], 1)

            def layer1(i, half):
                c = 2 * i + half
                pe.wait_ge(zt_ready, 2 * (c + 1))
                pe.wait_ge(ctx_loaded[half], 16 * (i + 1))
                for m in range(H1 // 128):
                    s = m // 2
                    if m % 2 == 0:
                        pe.wait_ge(mlp_moved[s], 3 * c + 1)
                    for b in range(NB):
                        last = nc.tensor.matmul(p_mlp[s][:, (m % 2) * CHUNK:(m % 2 + 1) * CHUNK],
                                                w1[:, b, m * 128:(m + 1) * 128], zt[:, half, b, :],
                                                start=(b == 0), stop=(b == NB - 1))
                    if m % 2 == 1:
                        last.then_inc(mlp_filled[s], 1)

            def layer2(i, half):
                c = 2 * i + half
                pe.wait_ge(h1_ready, H1 // 128 * (c + 1))
                pe.wait_ge(mlp_moved[0], 3 * c + 2)
                for m in range(H2 // 128):
                    for k in range(H1 // 128):
                        last = nc.tensor.matmul(p_mlp[0][:, m * CHUNK:(m + 1) * CHUNK], w2[:, k, m * 128:(m + 1) * 128],
                                                h1[:, k, :], start=(k == 0), stop=(k == H1 // 128 - 1))
                last.then_inc(mlp_filled[0], 1)

            def layer3(i, half):
                c = 2 * i + half
                pe.wait_ge(h2_ready, H2 // 128 * (c + 1))
                pe.wait_ge(mlp_moved[1], 3 * c + 2)
                for k in range(H2 // 128):
                    last = nc.tensor.matmul(p_mlp[1][0:1, 0:CHUNK], w3[:, k:k + 1], h2[:, k, :],
                                            start=(k == 0), stop=(k == H2 // 128 - 1))
                last.then_inc(mlp_filled[1], 1)

            def turn(i, last):
                transpose_tile(i, 0, 0)
                transpose_tile(i, 0, 1)
                gram_tile(i, 0, 0)
                gram_tile(i, 0, 1)
                onehot_chunk(i, 1, {1: lambda: pairs(i, 0), 3: lambda: layer1(i, 0), 4: lambda: layer2(i, 0), 5: lambda: layer3(i, 0)})
                if last:
                    for k in range(2):
                        transpose_tile(i, 1, k)
                        gram_tile(i, 1, k)
                    for stage in (pairs, layer1, layer2, layer3):
                        stage(i, 1)
                    return
                transpose_tile(i, 1, 0)
                transpose_tile(i, 1, 1)
                gram_tile(i, 1, 0)
                gram_tile(i, 1, 1)
                onehot_chunk(i + 1, 0, {1: lambda: pairs(i, 1), 3: lambda: layer1(i, 1), 4: lambda: layer2(i, 1), 5: lambda: layer3(i, 1)})

            onehot_chunk(0, 0, {})
            pe.wait_ge(ident_loaded, 16)
            pe.wait_ge(weights_loaded, 16 * NWEIGHTS)
            pe.wait_ge(pad_zeroed, 1)
            turn(0, False)
            with pe.Fori(1, TURNS - 1) as i:
                turn(i, False)
            turn(TURNS - 1, True)

        @block.scalar
        def _(act):
            act.dma_start(ident[:, :], a["ident"]).then_inc(ident_loaded, 16)

            def make_hi(t):
                act.wait_ge(raw_loaded[t % RAWS], 16 * (t // RAWS + 1))
                nc.scalar.copy(table_hi[:, t, :], raw[t % RAWS]).then_inc(hi_made, 1)

            def move_onehot(i, half, g):
                t0, n = ONEHOT_GROUPS[g]
                v = 2 * (t0 + n) - 1
                act.wait_ge(oh_used[v % OH_SLOTS], UNITS * (2 * i + half) + v // OH_SLOTS + 1)
                bank = bank_of_onehot(half, g)
                nc.scalar.copy(et_slots(et, NG + t0, n, 0, 2), bank[:, 0:n * CHUNK].rearrange("p (t k s) -> p t k s", t=n, k=2)
                               ).then_inc(et_moved, 1)

            def move_tile(i, half, k):
                for g, (s0, n) in enumerate(GATHER_GROUPS):
                    if g == NTB - 1:
                        act.wait_ge(tile_transposed[2 * half + k], i + 1)
                    else:
                        act.wait_ge(et_filled, (NTB - 1) * (4 * i + 2 * half + k) + g + 1)
                    nc.scalar.copy(et_slots(et, s0, n, k, 1), bank_of_tile(half, k, g)[:, 0:n * TILE].rearrange("p (t k s) -> p t k s", t=n, k=1)
                                   ).then_inc(et_moved, 1)

            def move_gram(i, half, k):
                if not (isinstance(i, int) and 2 * i + half == 0):
                    act.wait_ge(gram_turned[k], 2 * i + half)
                for b in range(GB):
                    act.wait_ge(gram_filled[b % 2], GRAMS * (4 * i + 2 * half + k) + b // 2 + 1)
                    for j in range(4):
                        src = p_gram[b % 2][32 * j:32 * j + 32, 0:16 * FEATS].rearrange("p (q c m) -> p q c m", q=4, c=4)[:, :, j, :]
                        dst = gram[32 * j:32 * j + 32, k, :].rearrange("p (m g) -> p g m", m=FEATS)[:, 4 * b:4 * b + 4, :]
                        last = nc.scalar.copy(dst, src)
                    last.then_inc(gram_moved[b % 2], 1)

            def relu1(i, half):
                for m in range(H1 // 128):
                    if m % 2 == 0:
                        act.wait_ge(mlp_filled[m // 2], 3 * (2 * i + half) + 2)
                    r = nc.scalar.activation(h1[:, m, :], p_mlp[m // 2][:, (m % 2) * CHUNK:(m % 2 + 1) * CHUNK],
                                             ACT.Relu, bias=b1[:, m:m + 1])
                    r.then_inc(h1_ready, 1)
                    if m % 2 == 1:
                        act.drain().then_inc(mlp_moved[m // 2], 1)

            def relu2(i, half):
                act.wait_ge(mlp_filled[0], 3 * (2 * i + half) + 3)
                for m in range(H2 // 128):
                    nc.scalar.activation(h2[:, m, :], p_mlp[0][:, m * CHUNK:(m + 1) * CHUNK],
                                         ACT.Relu, bias=b2[:, m:m + 1]).then_inc(h2_ready, 1)
                act.drain().then_inc(mlp_moved[0], 1)

            def after_onehot(i, half, mi, mhalf):
                move_onehot(i, half, 0)
                move_onehot(i, half, 1)
                relu1(mi, mhalf)
                relu2(mi, mhalf)
                for g in range(2, NOB):
                    move_onehot(i, half, g)

            def turn(i, last):
                move_tile(i, 0, 0)
                move_tile(i, 0, 1)
                move_gram(i, 0, 0)
                move_gram(i, 0, 1)
                after_onehot(i, 1, i, 0)
                if last:
                    for k in range(2):
                        move_tile(i, 1, k)
                        move_gram(i, 1, k)
                    relu1(i, 1)
                    relu2(i, 1)
                    return
                move_tile(i, 1, 0)
                move_tile(i, 1, 1)
                move_gram(i, 1, 0)
                move_gram(i, 1, 1)
                after_onehot(i + 1, 0, i, 1)

            for t in range(4):
                make_hi(t)
            for g in range(NOB):
                for t in (2 * g + 4, 2 * g + 5):
                    if t < NO:
                        make_hi(t)
                move_onehot(0, 0, g)
                if g == 0:
                    for dst, src in ((w1, "w1"), (w2, "w2"), (w3, "w3"), (b1, "b1"), (b2, "b2")):
                        act.dma_start(dst[:], a[src]).then_inc(weights_loaded, 16)
            act.wait_ge(weights_loaded, 16 * NWEIGHTS)
            turn(0, False)
            with act.Fori(1, TURNS - 1) as i:
                turn(i, False)
            turn(TURNS - 1, True)

        @block.vector
        def _(dve):
            nc.vector.memset(et[:, :, :].rearrange("p k (s f) -> p (k s) f", f=32)[:, :, FEATS:32], 0.0).then_inc(pad_zeroed, 1)
            dve.wait_ge(const_loaded, 16)

            def make_lo(t):
                dve.wait_ge(hi_made, t + 1)
                nc.vector.tensor_tensor(table_lo[:, t, :], raw[t % RAWS], table_hi[:, t, :].bitcast(fp32),
                                        ALU.subtract).then_inc(lo_made, 1)

            def build_unit(i, half, v):
                t, part = v // 2, v % 2
                s = v % OH_SLOTS
                if v == 0:
                    dve.wait_ge(bc_loaded, 16 * (2 * i + half + 1))
                n = UNITS * (2 * i + half) + v // OH_SLOTS
                if not (isinstance(n, int) and n == 0):
                    dve.wait_ge(oh_used[s], n)
                for k in range(HALF):
                    kk = part * HALF + k
                    last = nc.vector.tensor_scalar(onehot[:, s, k, :], ids_bc[:, t, :], rowno[:, kk:kk + 1], None, ALU.is_equal)
                last.then_inc(oh_built[s], 1)
                if v == 2 * NO - 1:
                    dve.drain().then_inc(chunk_built, 1)

            def turn_gram(i, half, k):
                c = 2 * i + half
                dve.wait_ge(gram_moved[0], GRAMS * (2 * c + k) + GRAMS)
                dve.wait_ge(gram_moved[1], GRAMS * (2 * c + k) + GRAMS)
                if not (isinstance(c, int) and c == 0):
                    dve.wait_ge(mlp_filled[k], 3 * c)
                nc.vector.transpose(samp[:, k, 0:FEATS * 32], gram[:, k, :]).then_inc(gram_turned[k], 1)
                dve.wait_ge(gram_turned[k], c + 1)
                nc.vector.tensor_copy(samp[:, k, FEATS * 32:SW], samp[:, k, 0:RADIUS * 32]).then_inc(samp_wrapped, 1)
                dve.wait_ge(samp_wrapped, 2 * c + k + 1)
                nc.vector.tensor_copy(prod[:, k, :].rearrange("p (n r) -> p n r", r=RADIUS), skewed(samp, k)).then_inc(prod_ready[k], 1)

            def move_pairs(i, half):
                c = 2 * i + half
                if not (isinstance(i, int) and i == 0):
                    dve.wait_ge(mlp_filled[1], 3 * (2 * i + half - 1) - 1)
                for k in range(2):
                    dve.wait_ge(mlp_filled[k], 3 * c + 1)
                    nc.vector.tensor_copy(zt[0:PAIRS, half, :, k * TILE:(k + 1) * TILE],
                                          p_mlp[k][0:PAIRS, 0:NB * TILE].rearrange("p (b s) -> p b s", b=NB)).then_inc(zt_ready, 1)
                    dve.drain().then_inc(mlp_moved[k], 1)

            def move_y(i, half):
                dve.wait_ge(mlp_filled[1], 3 * (2 * i + half) + 3)
                if not (isinstance(i, int) and i == 0):
                    dve.wait_ge(out_stored[half], 16 * i)
                nc.vector.tensor_copy(y_sb[0:1, half, :], p_mlp[1][0:1, 0:CHUNK]).then_inc(y_ready[half], 1)
                dve.drain().then_inc(mlp_moved[1], 1)

            def gram_and_onehot(i, half, mi, mhalf):
                turn_gram(mi, mhalf, 0)
                for v in range(2 * NO):
                    if v == 3:
                        turn_gram(mi, mhalf, 1)
                    if v == 6:
                        move_pairs(mi, mhalf)
                    if v == 14:
                        move_y(mi, mhalf)
                    build_unit(i, half, v)

            def turn(i, last):
                gram_and_onehot(i, 1, i, 0)
                if last:
                    turn_gram(i, 1, 0)
                    turn_gram(i, 1, 1)
                    move_pairs(i, 1)
                    move_y(i, 1)
                    return
                gram_and_onehot(i + 1, 0, i, 1)

            for t in range(NO):
                make_lo(t)
                build_unit(0, 0, 2 * t)
                build_unit(0, 0, 2 * t + 1)
            turn(0, False)
            with dve.Fori(1, TURNS - 1) as i:
                turn(i, False)
            turn(TURNS - 1, True)


def skewed(samp, k):
    v = samp[:, k, 32:]
    return bass.AP(v.tensor, v.offset, [v.ap[0], [33, FEATS], [32, RADIUS]])


def et_slots(et, s0, n, k, tiles):
    return et[:, k:k + tiles, :].rearrange("p k (s f) -> p f k s", f=32)[:, s0:s0 + n, :, :]


def kernel(**inputs):
    import concourse.bacc as bacc
    from concourse import mybir
    from concourse.bass_utils import run_bass_kernel_spmd

    x = {name: np.asarray(v) for name, v in inputs.items()}
    ids = x["ids"].reshape(BATCH // TILE, 4, 32, FEATS).transpose(0, 2, 1, 3).reshape(BATCH, FEATS)
    arrays = {f"tbl_{f}": x[f"tbl_{f}"] for f in GATHER_TABLES}
    arrays["ids_gather"] = np.ascontiguousarray(ids[:, GATHER_TABLES].reshape(BATCH // TILE, TILE, NG))
    arrays["ids_onehot"] = np.ascontiguousarray(ids[:, ONEHOT_TABLES].reshape(BATCH // CHUNK, CHUNK, NO).transpose(0, 2, 1))
    arrays["tables_onehot"] = np.stack([x[f"tbl_{f}"].reshape(KROWS, KCH * EMB) for f in ONEHOT_TABLES])
    ctx = np.zeros((NB * CTX_ROWS, BATCH), x["dense_ctx"].dtype)
    ctx[:CTX] = x["dense_ctx"].T
    arrays["ctx"] = np.ascontiguousarray(ctx.reshape(NB, CTX_ROWS, BATCH // CHUNK, CHUNK).transpose(2, 1, 0, 3))
    rows = pair_rows()
    w1 = np.zeros((NB, K1, H1), x["W_top1"].dtype)
    w1[rows >= 0] = x["W_top1"][rows[rows >= 0]]
    arrays["w1"] = np.ascontiguousarray(w1.transpose(1, 0, 2))
    arrays["w2"] = np.ascontiguousarray(x["W_top2"].reshape(H1 // 128, 128, H2).transpose(1, 0, 2))
    arrays["w3"] = np.ascontiguousarray(x["W_top3"].reshape(H2 // 128, 128).T)
    arrays["b1"] = np.ascontiguousarray(x["b_top1"].reshape(H1 // 128, 128).T)
    arrays["b2"] = np.ascontiguousarray(x["b_top2"].reshape(H2 // 128, 128).T)
    arrays["ident"] = np.eye(128, dtype=np.float32)
    arrays["rowno"] = np.arange(KROWS * KCH, dtype=np.float32).reshape(KROWS, KCH)

    nc = bacc.Bacc("TRN2", target_bir_lowering=False, num_devices=1)
    a = {n: nc.dram_tensor(f"in_{n}", v.shape, mybir.dt.from_np(v.dtype), kind="ExternalInput").ap() for n, v in arrays.items()}
    a["out"] = nc.dram_tensor("out_y", (BATCH // CHUNK, CHUNK), mybir.dt.float32, kind="ExternalOutput").ap()
    build(nc, a)
    r = run_bass_kernel_spmd(nc, [{f"in_{n}": v for n, v in arrays.items()}], core_ids=[0])
    return r.results[0]["out_y"].reshape(BATCH, 1)
```

```python
import numpy as np
import concourse.bass as bass
from concourse import mybir
from contextlib import ExitStack

BATCH = 2048
EMB = 128
CTX = 16
TABLE_ROWS = [1250, 1250, 125000, 1000, 1250, 12500, 12500, 1250, 12500, 1250, 12500, 12500, 1000, 1000,
              1000, 12500, 1250, 1250, 1000, 1000, 1000, 1000, 12500, 12500, 1250, 1250, 1000]
FEATS = len(TABLE_ROWS)
H1, H2 = 512, 256

SMALL = 1000
NO = 8
ONEHOT_TABLES = [f for f in range(FEATS) if TABLE_ROWS[f] == SMALL][:NO]
GATHER_TABLES = [f for f in range(FEATS) if f not in ONEHOT_TABLES]
NG = FEATS - NO
SLOTS = GATHER_TABLES + ONEHOT_TABLES
KROWS = 125
KCH = SMALL // KROWS

TILE = 128
CHUNK = 2 * TILE
CHUNKS = BATCH // CHUNK
PAIR = 2
TILES = PAIR * CHUNK // TILE

RADIUS = (FEATS - 1) // 2
MOVING = FEATS - 1
NB = 3
PAIRS = FEATS // NB * RADIUS
CTX_ROWS = 6
K1 = PAIRS + CTX_ROWS

def groups(total, count):
    sizes = [total // count + (g < total % count) for g in range(count)]
    return [(sum(sizes[:g]), sizes[g]) for g in range(count)]


GATHER_GROUPS = groups(NG, 5)


def pair_rows():
    iu = np.triu_indices(FEATS, k=1)
    row_of = {(a, b): k for k, (a, b) in enumerate(zip(*iu))}
    rows = np.full((NB, K1), -1)
    for b in range(NB):
        for q in range(PAIRS):
            n, r = b * (FEATS // NB) + q // RADIUS, 1 + q % RADIUS
            x, y = SLOTS[n], SLOTS[(n + r) % FEATS]
            rows[b, q] = row_of[(min(x, y), max(x, y))]
        for q in range(CTX_ROWS):
            if b * CTX_ROWS + q < CTX:
                rows[b, PAIRS + q] = len(iu[0]) + b * CTX_ROWS + q
    return rows


def build(nc, a):
    fp32, fp32r, i32 = mybir.dt.float32, mybir.dt.float32r, mybir.dt.int32
    ALU, ACT = mybir.AluOpType, mybir.ActivationFunctionType

    ctx = ExitStack()
    with ctx:
        def sb(name, shape, dt):
            return ctx.enter_context(nc.sbuf_tensor(name, shape, dt))

        def pb(name, shape, dt):
            return ctx.enter_context(nc.psum_tensor(name, shape, dt))

        def sem(name):
            return ctx.enter_context(nc.semaphore(name))

        def sems(name, n):
            return [sem(f"{name}{k}") for k in range(n)]

        SW = (FEATS + RADIUS) * 32
        OH_SLOTS = 4
        table_hi = sb("table_hi", [KROWS, NO, KCH * EMB], fp32r)
        table_lo = sb("table_lo", [KROWS, NO, KCH * EMB], fp32r)
        gath = sb("gath", [TILE, TILES, NG, EMB], fp32)
        et = sb("et", [EMB, 2, TILE * 32], fp32)
        onehot = sb("onehot", [KROWS, OH_SLOTS, 2, 2, CHUNK], fp32r)
        idx = sb("idx", [TILE, TILES, NG], i32)
        ids_bc = sb("ids_bc", [KROWS, NO, CHUNK], i32)
        gram = sb("gram", [128, 2, MOVING * 32], fp32)
        samp = sb("samp", [TILE, SW], fp32)
        prod = sb("prod", [TILE, 2, NB * PAIRS], fp32)
        zt = sb("zt", [K1, NB, CHUNK], fp32)
        zt_hi = sb("zt_hi", [K1, NB, CHUNK], fp32r)
        zt_lo = sb("zt_lo", [K1, NB, CHUNK], fp32r)
        h1 = sb("h1", [128, H1 // 128, CHUNK], fp32)
        h2 = sb("h2", [128, H2 // 128, CHUNK], fp32)
        y_sb = sb("y_sb", [1, 2, CHUNK], fp32)
        w1_hi = sb("w1_hi", [K1, NB, H1], fp32r)
        w1_lo = sb("w1_lo", [K1, NB, H1], fp32r)
        w2 = sb("w2", [128, H1 // 128, H2], fp32)
        w3 = sb("w3", [128, H2 // 128], fp32)
        b1 = sb("b1", [128, H1 // 128], fp32)
        b2 = sb("b2", [128, H2 // 128], fp32)
        ident = sb("ident", [128, 128], fp32)
        rowno = sb("rowno", [KROWS, KCH], fp32)
        late = gath[0:KROWS, 2:TILES, :, :].rearrange("p k s d -> p (k s d)")
        raw = [samp[0:KROWS, 0:KCH * EMB], gram[0:KROWS, :, :].rearrange("p k c -> p (k c)")[:, 0:KCH * EMB],
               h1[0:KROWS, :, :].rearrange("p m s -> p (m s)"), *(late[:, s * KCH * EMB:(s + 1) * KCH * EMB] for s in range(3))]
        RAWS = len(raw)
        w1_raw = gath[0:K1, 2:TILES, :, :].rearrange("p k s d -> p (k s d)")[:, 3 * KCH * EMB:3 * KCH * EMB + NB * H1]

        EB = 4
        p_et = [pb(f"p_et{s}", [128, 512], fp32) for s in range(EB)]
        p_gram = [pb(f"p_gram{s}", [128, 512], fp32) for s in range(2)]
        p_mlp = [pb(f"p_mlp{s}", [128, 512], fp32) for s in range(2)]

        idx_loaded = sems("idx_loaded", TILES)
        bc_loaded = sem("bc_loaded")
        bc_pair_loaded = sem("bc_pair_loaded")
        ctx_loaded = sem("ctx_loaded")
        raw_loaded = sems("raw_loaded", RAWS)
        rowno_loaded = sem("rowno_loaded")
        ident_loaded = sem("ident_loaded")
        distance_made = sem("distance_made")
        w1_loaded = sem("w1_loaded")
        weights_loaded = sem("weights_loaded")
        gathered = [sems(f"gathered{k}_", len(GATHER_GROUPS)) for k in range(TILES)]
        out_stored = sems("out_stored", 2)
        tiles_begun = sem("tiles_begun")
        hi_made = sem("hi_made")
        lo_made = sem("lo_made")
        w1_hi_made = sem("w1_hi_made")
        w1_lo_made = sem("w1_lo_made")
        pad_zeroed = sem("pad_zeroed")
        oh_built = sems("oh_built", OH_SLOTS)
        oh_used = sems("oh_used", OH_SLOTS)
        chunk_built = sem("chunk_built")
        tile_transposed = sems("tile_transposed", TILES)
        et_filled = sem("et_filled")
        et_moved = sems("et_moved", 2)
        gram_filled = sems("gram_filled", 2)
        gram_moved = sems("gram_moved", 2)
        gram_turned = sem("gram_turned")
        samp_ready = sem("samp_ready")
        prod_ready = sems("prod_ready", 2)
        mlp_filled = sems("mlp_filled", 2)
        zt_ready = sem("zt_ready")
        zt_hi_made = sem("zt_hi_made")
        zt_split = sem("zt_split")
        h1_ready = sem("h1_ready")
        h2_ready = sem("h2_ready")
        y_ready = sems("y_ready", 2)

        NWEIGHTS = 4
        ACT_UNIT = 2
        distance = [h2[0:KROWS, :, :], prod[0:KROWS, :, :].rearrange("p k q -> p (k q)")[:, 0:2 * CHUNK].rearrange("p (t s) -> p t s", t=2)]
        UNITS = NO * 2 // OH_SLOTS
        GB = TILE // 16
        GRAMS = GB // 2
        MLP_USES = 3

        NTB = len(GATHER_GROUPS)
        assert NO == 2 * EB == 8 and NTB == EB + 1
        EVEN, ODD = (NTB + 1) // 2, NTB // 2

        def moves_before(c, engine):
            return 2 + c * (2 * (EVEN, ODD)[engine] + 2)

        def bank_of_table(t):
            return 2 * (t // 4) + t % 2, (t // 2) % 2

        def bank_of_tile(k, g):
            return p_et[g % EB if k == 0 else 2 + g % 2]

        def number(h, p):
            return PAIR * h + p

        def before(h, p):
            return (h, 0) if p else (h - 1, 1)

        def after(h, p):
            return (h + 1, 0) if p else (h, 1)

        def onehot_bank_ready(eng, h, p, bank):
            u = 2 * (bank // 2) + 1
            eng.wait_ge(oh_used[(4 * u + 3) % OH_SLOTS], UNITS * number(h, p) + (4 * u + 3) // OH_SLOTS + 1)

        def onehot_bank(bank):
            t = 4 * (bank // 2) + bank % 2
            return (et_slots(et, NG + t, 3, 0, 2)[:, ::2, :, :],
                    p_et[bank][:, :].rearrange("p (t k s) -> p t k s", t=2, k=2))

        def transposes_ready(eng, h, p, k, g):
            if g == NTB - 1:
                eng.wait_ge(tile_transposed[2 * p + k], h + 1)
            else:
                eng.wait_ge(et_filled, (NTB - 1) * (2 * number(h, p) + k) + g + 1)

        def transposed(k, g):
            s0, n = GATHER_GROUPS[g]
            return (et_slots(et, s0, n, k, 1),
                    bank_of_tile(k, g)[:, 0:n * TILE].rearrange("p (t k s) -> p t k s", t=n, k=1))

        block = ctx.enter_context(nc.Block())

        @block.sync
        def _(sp):
            def load_idx(h, p, k):
                tile = 2 * p + k
                sp.dma_start(idx[:, tile, :], a["ids_gather"][bass.ds(h * TILES + tile, 1), :, :].rearrange("o p f -> (o p) f")
                             ).then_inc(idx_loaded[tile], 16)

            def load_bc(h, p):
                sp.dma_start(ids_bc[:, :, :], a["ids_onehot"][bass.ds(number(h, p), 1), :, :].to_broadcast([KROWS, NO, CHUNK])
                             ).then_inc(bc_loaded, 16)

            def load_first_bc(t, n, loaded):
                sp.dma_start(ids_bc[:, t:t + n, :], a["ids_onehot"][0:1, t:t + n, :].to_broadcast([KROWS, n, CHUNK])).then_inc(loaded, 16)

            def load_ctx(h, p):
                sp.dma_start(zt[PAIRS:K1, :, :], a["ctx"][bass.ds(number(h, p), 1), :, :, :].rearrange("o q b s -> (o q) b s")
                             ).then_inc(ctx_loaded, 16)

            def load_raw(t):
                if t >= RAWS:
                    sp.wait_ge(lo_made, t - RAWS + 1)
                sp.dma_start(raw[t % RAWS], a["tables_onehot"][t]).then_inc(raw_loaded[t % RAWS], 16)

            def store_y(h, p):
                sp.wait_ge(y_ready[p], h + 1)
                sp.dma_start(a["out"][bass.ds(number(h, p), 1), :], y_sb[0:1, p, :]).then_inc(out_stored[p], 16)

            def during(h, p, idx_ahead, bc_ahead, first=False):
                if idx_ahead:
                    sp.wait_ge(tile_transposed[2 * p], h + 1)
                    load_idx(h + 1, p, 0)
                if not first:
                    sp.wait_ge(zt_split, number(h, p))
                    load_ctx(h, p)
                    store_y(*before(h, p))
                if idx_ahead:
                    sp.wait_ge(tile_transposed[2 * p + 1], h + 1)
                    load_idx(h + 1, p, 1)
                if bc_ahead:
                    sp.wait_ge(chunk_built, number(h, p) + 2)
                    load_bc(h + 1, p)

            for p in range(PAIR):
                sp.sem_inc(out_stored[p], 16)
            load_idx(0, 0, 0)
            load_first_bc(0, 2, bc_pair_loaded)
            load_raw(0)
            load_raw(1)
            load_raw(2)
            load_idx(0, 0, 1)
            load_raw(3)
            load_first_bc(2, NO - 2, bc_loaded)
            for t in range(4, NO):
                load_raw(t)
            sp.dma_start(w1_raw, a["w1"].rearrange("p b m -> p (b m)")).then_inc(w1_loaded, 16)
            for k in range(2):
                load_idx(0, 1, k)
            sp.wait_ge(chunk_built, 1)
            sp.wait_ge(oh_built[ACT_UNIT % OH_SLOTS], UNITS)
            load_bc(0, 1)
            load_ctx(0, 0)
            during(0, 0, True, True, first=True)
            with sp.Fori(0, CHUNKS // PAIR - 2) as h:
                during(h, 1, True, True)
                during(h + 1, 0, True, True)
            during(CHUNKS // PAIR - 2, 1, True, True)
            during(CHUNKS // PAIR - 1, 0, False, False)
            during(CHUNKS // PAIR - 1, 1, False, False)
            store_y(CHUNKS // PAIR - 1, 1)
            for p in range(PAIR):
                sp.wait_ge(out_stored[p], 16 * (CHUNKS // PAIR + 1))

        @block.gpsimd
        def _(pool):
            def gather_tiles(h):
                for tile in range(TILES):
                    pool.wait_ge(idx_loaded[tile], 16 * (h + 1))
                    if not isinstance(h, int):
                        pool.wait_ge(tile_transposed[tile], h)
                    elif tile == 2:
                        pool.wait_ge(lo_made, NO)
                        pool.wait_ge(w1_lo_made, 1)
                    pool.sem_inc(tiles_begun, 1)
                    for g, (s0, n) in enumerate(GATHER_GROUPS):
                        for s in range(s0, s0 + n):
                            pool.indirect_dma_start(
                                gath[:, tile, s, :], None, a[f"tbl_{GATHER_TABLES[s]}"],
                                bass.IndirectOffsetOnAxis(ap=idx[:, tile, s:s + 1], axis=0),
                            ).then_inc(gathered[tile][g], 16)

            gather_tiles(0)
            with pool.Fori(1, CHUNKS // PAIR) as h:
                gather_tiles(h)

        @block.tensor
        def _(pe):
            def onehot_tables(h, p, u):
                c = number(h, p)
                if isinstance(c, int) and c == 0:
                    pe.wait_ge(lo_made, 2 * u + 2)
                elif u % 2 == 0:
                    pe.wait_ge(et_moved[0], moves_before(c - 1, 0) + EVEN * (1 + u // 2))
                    pe.wait_ge(et_moved[1], moves_before(c - 1, 1) + (1 if u == 0 else 2 * ODD))
                for part in range(4):
                    v = 4 * u + part
                    pe.wait_ge(oh_built[v % OH_SLOTS], UNITS * c + v // OH_SLOTS + 1)
                    for k in range(2):
                        kk = 2 * part + k
                        for t in (0, 1):
                            bank, half = bank_of_table(2 * u + t)
                            for tab in (table_hi, table_lo):
                                last = nc.tensor.matmul(p_et[bank][:, half * CHUNK:(half + 1) * CHUNK],
                                                        tab[:, 2 * u + t, kk * EMB:(kk + 1) * EMB], onehot[:, v % OH_SLOTS, k, t, :],
                                                        start=(kk == 0 and tab is table_hi), stop=(kk == KCH - 1 and tab is table_lo))
                    last.then_inc(oh_used[v % OH_SLOTS], 1)

            def transpose_batch(h, p, k, g):
                c, tile = number(h, p), 2 * p + k
                s0, n = GATHER_GROUPS[g]
                pe.wait_ge(gathered[tile][g], 16 * n * (h + 1))
                engine, n_moved = ((0, -1), (0, 0), (1, -1), (1, 0), (0, 1))[g] if k == 0 else ((0, 2), (1, 2), (0, 4), (1, 3), (0, 5))[g]
                pe.wait_ge(et_moved[engine], moves_before(c, engine) + n_moved)
                for s in range(s0, s0 + n):
                    last = nc.tensor.transpose(bank_of_tile(k, g)[:, (s - s0) * TILE:(s - s0 + 1) * TILE],
                                               gath[:, tile, s, :], ident[:, :])
                last.then_inc(tile_transposed[tile] if g == NTB - 1 else et_filled, 1)

            def gram_batch(h, p, k, b):
                c = number(h, p)
                if b == 0:
                    for engine in range(2):
                        pe.wait_ge(et_moved[engine], moves_before(c, engine) + (k + 1) * (EVEN, ODD)[engine])
                uses = GRAMS * (2 * c + k) + b // 2
                if not (isinstance(uses, int) and uses == 0):
                    pe.wait_ge(gram_moved[b % 2], uses)
                for q in range(4):
                    stat = et[:, k, 128 * (4 * b + q):128 * (4 * b + q + 1)]
                    mov = stat.rearrange("p (j f) -> p j f", f=32)[:, :, 0:MOVING]
                    last = nc.tensor.matmul(p_gram[b % 2][:, q * 4 * MOVING:(q + 1) * 4 * MOVING], stat, mov, start=True, stop=True)
                last.then_inc(gram_filled[b % 2], 1)

            def pairs(h, p, k):
                c = number(h, p)
                pe.wait_ge(prod_ready[k], c + 1)
                for b in range(NB):
                    last = nc.tensor.transpose(p_mlp[k][0:PAIRS, b * TILE:(b + 1) * TILE],
                                               prod[:, k, b * PAIRS:(b + 1) * PAIRS], ident[:, :])
                last.then_inc(mlp_filled[k], 1)

            def layer1(h, p):
                c = number(h, p)
                pe.wait_ge(zt_split, c + 1)
                for m in range(H1 // 128):
                    for b in range(NB):
                        for n, (w, z) in enumerate(((w1_hi, zt_hi), (w1_hi, zt_lo), (w1_lo, zt_hi))):
                            last = nc.tensor.matmul(p_mlp[m // 2][:, (m % 2) * CHUNK:(m % 2 + 1) * CHUNK],
                                                    w[:, b, m * 128:(m + 1) * 128], z[:, b, :],
                                                    start=(b == 0 and n == 0), stop=(b == NB - 1 and n == 2))
                    if m % 2 == 1:
                        last.then_inc(mlp_filled[m // 2], 1)

            def layer2(h, p):
                c = number(h, p)
                pe.wait_ge(h1_ready, H1 // 128 * (c + 1))
                for m in range(H2 // 128):
                    for k in range(H1 // 128):
                        last = nc.tensor.matmul(p_mlp[0][:, m * CHUNK:(m + 1) * CHUNK], w2[:, k, m * 128:(m + 1) * 128],
                                                h1[:, k, :], start=(k == 0), stop=(k == H1 // 128 - 1))
                last.then_inc(mlp_filled[0], 1)

            def layer3(h, p):
                c = number(h, p)
                pe.wait_ge(h2_ready, H2 // 128 * (c + 1))
                for k in range(H2 // 128):
                    last = nc.tensor.matmul(p_mlp[1][0:1, 0:CHUNK], w3[:, k:k + 1], h2[:, k, :],
                                            start=(k == 0), stop=(k == H2 // 128 - 1))
                last.then_inc(mlp_filled[1], 1)

            def chunk(h, p, first=False, final=False):
                prior, nxt = before(h, p), after(h, p)
                for g in range(2 if first else 0, NTB):
                    transpose_batch(h, p, 0, g)
                if not first:
                    for k in range(2):
                        pairs(*prior, k)
                for b in range(GB):
                    gram_batch(h, p, 0, b)
                    if b == 3 and not first:
                        layer1(*prior)
                    if b in (2, 5) and not final:
                        onehot_tables(*nxt, b // 4)
                    if b >= GB - NTB:
                        transpose_batch(h, p, 1, b - (GB - NTB))
                if not first:
                    layer2(*prior)
                for b in range(GB):
                    gram_batch(h, p, 1, b)
                    if b == 1 and not final:
                        onehot_tables(*nxt, 2)
                    if b == 3 and not first:
                        layer3(*prior)
                    if b == 5 and final:
                        pairs(h, p, 0)
                if not final:
                    onehot_tables(*nxt, 3)

            for u in range(3):
                onehot_tables(0, 0, u)
            pe.wait_ge(ident_loaded, 16)
            for g in range(2):
                transpose_batch(0, 0, 0, g)
            onehot_tables(0, 0, 3)
            pe.wait_ge(pad_zeroed, 1)
            chunk(0, 0, first=True)
            pe.wait_ge(weights_loaded, 16 * NWEIGHTS)
            pe.wait_ge(w1_lo_made, 1)
            with pe.Fori(0, CHUNKS // PAIR - 1) as h:
                chunk(h, 1)
                chunk(h + 1, 0)
            end = (CHUNKS // PAIR - 1, 1)
            chunk(*end, final=True)
            pairs(*end, 1)
            layer1(*end)
            layer2(*end)
            layer3(*end)

        @block.scalar
        def _(act):
            act.dma_start(rowno[:, :], a["rowno"]).then_inc(rowno_loaded, 16)
            act.dma_start(ident[:, :], a["ident"]).then_inc(ident_loaded, 16)

            def make_hi(t):
                act.wait_ge(raw_loaded[t % RAWS], 16 * (t // RAWS + 1))
                nc.scalar.copy(table_hi[:, t, :], raw[t % RAWS]).then_inc(hi_made, 1)

            def move_onehot(h, p, bank):
                onehot_bank_ready(act, h, p, bank)
                nc.scalar.copy(*onehot_bank(bank)).then_inc(et_moved[0], 1)

            def move_transposed(h, p, k, g):
                transposes_ready(act, h, p, k, g)
                nc.scalar.copy(*transposed(k, g)).then_inc(et_moved[0], 1)

            def move_gram(h, p, k, b):
                c = number(h, p)
                act.wait_ge(gram_filled[b % 2], GRAMS * (2 * c + k) + b // 2 + 1)
                for j in range(4):
                    src = p_gram[b % 2][32 * j:32 * j + 32, 0:16 * MOVING].rearrange("p (q c m) -> p q c m", q=4, c=4)[:, :, j, :]
                    dst = gram[32 * j:32 * j + 32, k, :].rearrange("p (m g) -> p g m", m=MOVING)[:, 4 * b:4 * b + 4, :]
                    last = nc.scalar.copy(dst, src)
                last.then_inc(gram_moved[b % 2], 1)

            def pick_pairs(h, p, k):
                act.wait_ge(samp_ready, 2 * number(h, p) + k + 1)
                nc.scalar.copy(prod[:, k, :].rearrange("p (n r) -> p n r", r=RADIUS), skewed(samp)).then_inc(prod_ready[k], 1)

            def make_zt_hi(h, p):
                c = number(h, p)
                act.wait_ge(ctx_loaded, 16 * (c + 1))
                act.wait_ge(zt_ready, 2 * (c + 1))
                nc.scalar.copy(zt_hi[:, :, :], zt[:, :, :]).then_inc(zt_hi_made, 1)

            def relu1(h, p):
                for m in range(H1 // 128):
                    if m % 2 == 0:
                        act.wait_ge(mlp_filled[m // 2], MLP_USES * number(h, p) + 2)
                    nc.scalar.activation(h1[:, m, :], p_mlp[m // 2][:, (m % 2) * CHUNK:(m % 2 + 1) * CHUNK],
                                         ACT.Relu, bias=b1[:, m:m + 1]).then_inc(h1_ready, 1)

            def relu2(h, p):
                act.wait_ge(mlp_filled[0], MLP_USES * number(h, p) + 3)
                for m in range(H2 // 128):
                    nc.scalar.activation(h2[:, m, :], p_mlp[0][:, m * CHUNK:(m + 1) * CHUNK],
                                         ACT.Relu, bias=b2[:, m:m + 1]).then_inc(h2_ready, 1)

            def chunk(h, p, first=False, final=False):
                prior = before(h, p)
                for g in range(0, NTB, 2):
                    move_transposed(h, p, 0, g)
                for b in range(GB):
                    move_gram(h, p, 0, b)
                    if b == 1 and not first:
                        make_zt_hi(*prior)
                    if b == 2 and first:
                        act.wait_ge(w1_loaded, 16)
                        nc.scalar.copy(w1_hi[:, :, :].rearrange("p b m -> p (b m)"), w1_raw).then_inc(w1_hi_made, 1)
                    if b == 5 and not first:
                        relu1(*prior)
                    if b >= GB - NTB and (b - (GB - NTB)) % 2 == 0:
                        move_transposed(h, p, 1, b - (GB - NTB))
                pick_pairs(h, p, 0)
                if not first:
                    relu2(*prior)
                for b in range(GB):
                    move_gram(h, p, 1, b)
                if not final:
                    for bank in (0, 1):
                        move_onehot(*after(h, p), bank)
                pick_pairs(h, p, 1)

            def build_onehot(v):
                t, s = 2 * (v // 4), v % OH_SLOTS
                if v // OH_SLOTS > 0:
                    act.wait_ge(oh_used[s], v // OH_SLOTS)
                    act.wait_ge(oh_built[s], v // OH_SLOTS)
                for k in range(2):
                    kk = 2 * (v % 4) + k
                    nc.scalar.activation(distance[k], ids_bc[:, t:t + 2, :], ACT.Abs, bias=rowno[:, kk:kk + 1], scale=-1.0).then_inc(distance_made, 1)
                for k in range(2):
                    act.wait_ge(distance_made, 2 * (v // 4) + k + 1)
                    last = nc.scalar.activation(onehot[:, s, k, :, :], distance[k], ACT.Relu, bias=1.0, scale=-1.0)
                last.then_inc(oh_built[s], 1)

            for t in range(NO):
                make_hi(t)
                if t == 3:
                    act.wait_ge(rowno_loaded, 16)
                    act.wait_ge(bc_pair_loaded, 16)
                    build_onehot(ACT_UNIT)
                if t == 4:
                    act.wait_ge(bc_loaded, 16)
                    build_onehot(4 + ACT_UNIT)
            build_onehot(8 + ACT_UNIT)
            for bank in (0, 1):
                move_onehot(0, 0, bank)
            build_onehot(12 + ACT_UNIT)
            for dst, src in ((w2, "w2"), (w3, "w3"), (b1, "b1"), (b2, "b2")):
                act.dma_start(dst[:], a[src]).then_inc(weights_loaded, 16)
            chunk(0, 0, first=True)
            act.wait_ge(weights_loaded, 16 * NWEIGHTS)
            with act.Fori(0, CHUNKS // PAIR - 1) as h:
                chunk(h, 1)
                chunk(h + 1, 0)
            end = (CHUNKS // PAIR - 1, 1)
            chunk(*end, final=True)
            make_zt_hi(*end)
            relu1(*end)
            relu2(*end)

        @block.vector
        def _(dve):
            nc.vector.memset(et[:, :, :].rearrange("p k (s f) -> p (k s) f", f=32)[:, :, FEATS:32], 0.0).then_inc(pad_zeroed, 1)
            dve.wait_ge(rowno_loaded, 16)

            def make_lo(t):
                dve.wait_ge(hi_made, t + 1)
                nc.vector.tensor_tensor(table_lo[:, t, :], raw[t % RAWS], table_hi[:, t, :].bitcast(fp32),
                                        ALU.subtract).then_inc(lo_made, 1)

            def build_onehot(h, p, v):
                c, t, s = number(h, p), 2 * (v // 4), v % OH_SLOTS
                if isinstance(c, int) and c == 0:
                    if v == 0:
                        dve.wait_ge(bc_pair_loaded, 16)
                    elif v == 4:
                        dve.wait_ge(bc_loaded, 16)
                elif v == 0:
                    dve.wait_ge(bc_loaded, 16 * (c + 1))
                uses = UNITS * c + v // OH_SLOTS
                if not (isinstance(uses, int) and uses == 0):
                    dve.wait_ge(oh_used[s], uses)
                kk = 2 * (v % 4)
                shape = [KROWS, 2, 2, CHUNK]
                nc.vector.tensor_tensor(onehot[:, s, :, :, :], ids_bc[:, t:t + 2, :].unsqueeze(1).to_broadcast(shape),
                                        rowno[:, kk:kk + 2].unsqueeze(2).unsqueeze(3).to_broadcast(shape), ALU.is_equal).then_inc(oh_built[s], 1)
                if v == 2 * NO - 1:
                    dve.drain().then_inc(chunk_built, 1)

            def move_onehot(h, p, bank):
                onehot_bank_ready(dve, h, p, bank)
                nc.vector.tensor_copy(*onehot_bank(bank)).then_inc(et_moved[1], 1)

            def move_transposed(h, p, k, g):
                transposes_ready(dve, h, p, k, g)
                nc.vector.tensor_copy(*transposed(k, g)).then_inc(et_moved[1], 1)

            def turn_gram(h, p, k):
                c = number(h, p)
                if not (isinstance(c, int) and c == 0 and k == 0):
                    bh, bp = (h, p) if k == 1 else before(h, p)
                    dve.wait_ge(prod_ready[1 - k], number(bh, bp) + 1)
                for s in range(2):
                    dve.wait_ge(gram_moved[s], GRAMS * (2 * c + k + 1))
                nc.vector.transpose(samp[:, 0:MOVING * 32], gram[:, k, :]).then_inc(gram_turned, 1)
                nc.vector.transpose(samp[:, FEATS * 32:SW], gram[:, k, 0:RADIUS * 32])
                dve.wait_ge(gram_turned, 2 * c + k + 1)
                nc.vector.tensor_copy(samp[:, MOVING * 32 + MOVING - RADIUS:MOVING * 32 + MOVING],
                                      samp[:, 0:MOVING * 32].rearrange("p (m n) -> p m n", n=32)[:, MOVING - RADIUS:MOVING, MOVING]).then_inc(samp_ready, 1)

            def move_pairs(h, p, k):
                dve.wait_ge(mlp_filled[k], MLP_USES * number(h, p) + 1)
                nc.vector.tensor_copy(zt[0:PAIRS, :, k * TILE:(k + 1) * TILE],
                                      p_mlp[k][0:PAIRS, 0:NB * TILE].rearrange("p (b s) -> p b s", b=NB)).then_inc(zt_ready, 1)

            def make_zt_lo(h, p):
                dve.wait_ge(zt_hi_made, number(h, p) + 1)
                nc.vector.tensor_tensor(zt_lo[:, :, :], zt[:, :, :], zt_hi[:, :, :].bitcast(fp32), ALU.subtract).then_inc(zt_split, 1)

            def move_y(h, p):
                dve.wait_ge(mlp_filled[1], MLP_USES * number(h, p) + 3)
                dve.wait_ge(out_stored[p], 16 * (h + 1))
                nc.vector.tensor_copy(y_sb[0:1, p, :], p_mlp[1][0:1, 0:CHUNK]).then_inc(y_ready[p], 1)

            def chunk(h, p, first=False, final=False):
                prior, nxt = before(h, p), after(h, p)

                def build(*units):
                    if not final:
                        for v in units:
                            build_onehot(*nxt, v)

                for g in range(1, NTB, 2):
                    move_transposed(h, p, 0, g)
                build(0)
                if not first:
                    move_pairs(*prior, 0)
                build(1)
                if not first:
                    move_pairs(*prior, 1)
                build(2, 3)
                if not first:
                    make_zt_lo(*prior)
                build(4, 5, 6, 7)
                if first:
                    dve.wait_ge(w1_hi_made, 1)
                    nc.vector.tensor_tensor(w1_lo[:, :, :].rearrange("p b m -> p (b m)"), w1_raw,
                                            w1_hi[:, :, :].rearrange("p b m -> p (b m)").bitcast(fp32), ALU.subtract).then_inc(w1_lo_made, 1)
                move_transposed(h, p, 1, 1)
                build(8, 9)
                move_transposed(h, p, 1, 3)
                build(10, 11)
                turn_gram(h, p, 0)
                build(12, 13, 14, 15)
                if not first:
                    move_y(*prior)
                if final:
                    move_pairs(h, p, 0)
                turn_gram(h, p, 1)
                if not final:
                    for bank in (2, 3):
                        move_onehot(*nxt, bank)

            for v in range(ACT_UNIT):
                build_onehot(0, 0, v)
            for u in range(NO // 2):
                make_lo(2 * u)
                make_lo(2 * u + 1)
                for v in range(4 * u, 4 * u + 4):
                    if v >= ACT_UNIT and v % 4 != ACT_UNIT:
                        build_onehot(0, 0, v)
            for bank in (2, 3):
                move_onehot(0, 0, bank)
            chunk(0, 0, first=True)
            with dve.Fori(0, CHUNKS // PAIR - 1) as h:
                chunk(h, 1)
                chunk(h + 1, 0)
            end = (CHUNKS // PAIR - 1, 1)
            chunk(*end, final=True)
            move_pairs(*end, 1)
            make_zt_lo(*end)
            move_y(*end)


def skewed(samp):
    v = samp[:, 32:]
    return bass.AP(v.tensor, v.offset, [v.ap[0], [33, FEATS], [32, RADIUS]])


def et_slots(et, s0, n, k, tiles):
    return et[:, k:k + tiles, :].rearrange("p k (s f) -> p f k s", f=32)[:, s0:s0 + n, :, :]


def kernel(**inputs):
    import concourse.bacc as bacc
    from concourse import mybir
    from concourse.bass_utils import run_bass_kernel_spmd

    x = {name: np.asarray(v) for name, v in inputs.items()}
    ids = x["ids"].reshape(BATCH // TILE, 4, 32, FEATS).transpose(0, 2, 1, 3).reshape(BATCH, FEATS)
    arrays = {f"tbl_{f}": x[f"tbl_{f}"] for f in GATHER_TABLES}
    arrays["ids_gather"] = np.ascontiguousarray(ids[:, GATHER_TABLES].reshape(BATCH // TILE, TILE, NG))
    arrays["ids_onehot"] = np.ascontiguousarray(ids[:, ONEHOT_TABLES].reshape(BATCH // CHUNK, CHUNK, NO).transpose(0, 2, 1))
    arrays["tables_onehot"] = np.stack([x[f"tbl_{f}"].reshape(KROWS, KCH * EMB) for f in ONEHOT_TABLES])
    ctx = np.zeros((NB * CTX_ROWS, BATCH), x["dense_ctx"].dtype)
    ctx[:CTX] = x["dense_ctx"].T
    arrays["ctx"] = np.ascontiguousarray(ctx.reshape(NB, CTX_ROWS, BATCH // CHUNK, CHUNK).transpose(2, 1, 0, 3))
    rows = pair_rows()
    w1 = np.zeros((NB, K1, H1), x["W_top1"].dtype)
    w1[rows >= 0] = x["W_top1"][rows[rows >= 0]]
    arrays["w1"] = np.ascontiguousarray(w1.transpose(1, 0, 2))
    arrays["w2"] = np.ascontiguousarray(x["W_top2"].reshape(H1 // 128, 128, H2).transpose(1, 0, 2))
    arrays["w3"] = np.ascontiguousarray(x["W_top3"].reshape(H2 // 128, 128).T)
    arrays["b1"] = np.ascontiguousarray(x["b_top1"].reshape(H1 // 128, 128).T)
    arrays["b2"] = np.ascontiguousarray(x["b_top2"].reshape(H2 // 128, 128).T)
    arrays["ident"] = np.eye(128, dtype=np.float32)
    arrays["rowno"] = np.arange(KROWS * KCH, dtype=np.float32).reshape(KROWS, KCH)

    nc = bacc.Bacc("TRN2", target_bir_lowering=False, num_devices=1)
    a = {n: nc.dram_tensor(f"in_{n}", v.shape, mybir.dt.from_np(v.dtype), kind="ExternalInput").ap() for n, v in arrays.items()}
    a["out"] = nc.dram_tensor("out_y", (BATCH // CHUNK, CHUNK), mybir.dt.float32, kind="ExternalOutput").ap()
    build(nc, a)
    r = run_bass_kernel_spmd(nc, [{f"in_{n}": v for n, v in arrays.items()}], core_ids=[0])
    return r.results[0]["out_y"].reshape(BATCH, 1)
```
